# Optimizing a Trainium2 kernel written in Bass

```python
import numpy as np
import jax
import jax.numpy as jnp

def _softmax(x, axis=-1):
    return jax.nn.softmax(x, axis=axis)

def _gelu(x):
    return jax.nn.gelu(x, approximate=True)

def _silu(x):
    return jax.nn.silu(x)

def _sigmoid(x):
    return jax.nn.sigmoid(x)

def _layernorm(x, axis=-1, eps=1e-05):
    m = jnp.mean(x, axis=axis, keepdims=True)
    v = jnp.var(x, axis=axis, keepdims=True)
    return (x - m) / jnp.sqrt(v + eps)

def _scatter_add(tgt, idx, src, axis=0):
    return tgt.at[idx].add(src)

def _segment_sum(src, seg, n):
    return jax.ops.segment_sum(src, seg, n)
kernel_name = 'mk_rec_standalone_d1_rec_r8_6602d1'

def setup_inputs(seed: int=0):
    np.random.seed(seed)
    _w = jnp.asarray

    def _rec_inputs():
        import jax
        import jax.numpy as jnp
        _rk = jax.random.key(seed)
        r_x = 7.22013e-05 + 1.00017 * jax.random.normal(jax.random.fold_in(_rk, 1), (2048, 32, 64), jnp.float32)
        return r_x
    r_x = _rec_inputs()

    def _L0_rec_setup():
        import jax, jax.numpy as jnp
        import numpy as np
        key = jax.random.key(seed)
        k1, k2 = jax.random.split(key)
        B, F, D = (512, 32, 64)
        P = F * (F - 1) // 2
        x = jax.random.normal(k1, (B, F, D), dtype=jnp.float32)
        W = jax.random.normal(k2, (P, D, D), dtype=jnp.float32) * (1.0 / np.sqrt(D))
        return {'x': x, 'W': W}
    _L0_rec_all = _L0_rec_setup()
    _L0_rec_in = {k: v for k, v in _L0_rec_all.items() if k in ('W',)}
    del _L0_rec_all
    return {'r_x': r_x, 'L0_rec_W': _L0_rec_in['W']}

def reference(r_x, L0_rec_W):
    import jax
    import jax.numpy as jnp

    def _L0_rec_ref(x, W):
        import jax, jax.numpy as jnp
        import numpy as np
        F = x.shape[1]
        idx_i, idx_j = np.triu_indices(F, k=1)
        xi = x[:, idx_i, :]
        xj = x[:, idx_j, :]
        left = jnp.einsum('bpd,pde->bpe', xi, W)
        out = jnp.sum(left * xj, axis=-1)
        return out
    y = _L0_rec_ref(r_x, L0_rec_W)
    return y

_drawn_inputs = setup_inputs


def setup_inputs(seed=0):
    import zlib

    import numpy as np

    out = dict(_drawn_inputs(seed))
    spreads = {}
    factors = {}
    for name, (base, spread) in spreads.items():
        noise = np.random.default_rng([zlib.crc32(name.encode()), seed]).standard_normal(out[name].shape)
        drawn = base * np.exp(spread * noise) if base else spread * noise
        out[name] = jnp.asarray(drawn.astype(out[name].dtype))
    for name, factor in factors.items():
        out[name] = (out[name] * factor).astype(out[name].dtype)
    return out
```

```python
from contextlib import ExitStack

import numpy as np

import concourse.bass as bass
from concourse import mybir

F32 = mybir.dt.float32
F32R = mybir.dt.float32r
ALU = mybir.AluOpType

BATCH, FIELDS, DIM = 2048, 32, 64
PAIRS = FIELDS * (FIELDS - 1) // 2
P = 128
COLS = 512
HALVES = 2
TILE = HALVES * COLS
TILES = BATCH // TILE
CHUNKS = FIELDS // 2
ROUNDS = CHUNKS // 2
STEPS = CHUNKS
GROUP = 4
GROUPS = STEPS // GROUP
GCOLS = GROUP * 2 * P
BATCHES = GROUPS * HALVES
RSTEPS = STEPS * HALVES
ALL_ROUNDS = TILES * ROUNDS
UNITS = 4
FIRST_UNITS = 2
RING = 2 * GROUP
BUFFERS = 3
LEAD = BUFFERS
OUT_ROWS = 4 * 2 * (2 * STEPS // 4)


def left_buffers():
    turn = [0] + [-1 if LEAD <= s < LEAD + 4 else 1 for s in range(1, RSTEPS)]
    buffers = [sum(turn[:s + 1]) % BUFFERS for s in range(RSTEPS)]
    ages = [next(d for d in range(1, RSTEPS) if buffers[s - d] == buffers[s]) for s in range(RSTEPS)]
    return buffers, ages


LEFT_BUFFER, LEFT_AGE = left_buffers()


def round_blocks(u):
    found = []
    for n in range(STEPS - 1):
        t = u + n + 1
        a, c = (u, t) if t < CHUNKS else (CHUNKS - 1 - u, 2 * CHUNKS - 1 - t)
        found += [(2 * a + b, [2 * c, 2 * c + 1]) for b in range(2)]
    return found + [(2 * a + 1, [2 * a]) for a in (u, CHUNKS - 1 - u)]


def bilinear_kernel(nc, xT, w, out):
    x_chunks = xT.rearrange("(c p) b -> p c b", p=P)

    with ExitStack() as ctx:
        def sb(name, shape, dt=F32):
            return ctx.enter_context(nc.sbuf_tensor(name, shape, dt))

        def sem(name):
            return ctx.enter_context(nc.semaphore(name))

        x_nat = sb("x_nat", [P, CHUNKS, TILE])
        x_raw = sb("x_raw", [P, 2, TILE])
        x_split = sb("x_split", [P, 2 * UNITS, TILE], F32R)
        w_raw = sb("w_raw", [P, 2, GCOLS])
        w_hi = sb("w_hi", [P, 2, GCOLS], F32R)
        w_lo = sb("w_lo", [P, 2, GCOLS], F32R)
        prod = sb("prod", [P, RING, 2, COLS])
        out_rows = sb("out_rows", [P, HALVES, COLS])
        ones = sb("ones", [P, 62])
        left = ctx.enter_context(nc.psum_tensor("left", [P, BUFFERS, 2, COLS], F32))
        sums = ctx.enter_context(nc.psum_tensor("sums", [P, HALVES, COLS], F32))

        nat_in = [sem(f"nat_in{c}") for c in range(CHUNKS)]
        x_in = [sem(f"x_in{k}") for k in range(2)]
        w_in = [sem(f"w_in{k}") for k in range(2)]
        ones_zero = sem("ones_zero")
        ones_ready = sem("ones_ready")
        x_hi = sem("x_hi")
        x_first = sem("x_first")
        x_ready = sem("x_ready")
        w_hi_done = sem("w_hi_done")
        w_ready = sem("w_ready")
        left_ready = sem("left_ready")
        prod_ready = sem("prod_ready")
        summed = sem("summed")
        rows_out = sem("rows_out")
        stored = sem("stored")

        block = ctx.enter_context(nc.Block())

        def second(u, n):
            return (u + (n + 1)) // CHUNKS if n >= STEPS // 2 else 0

        def set_ahead(engine, start):
            if not isinstance(start, int):
                engine.compute_val(start * 4)
            return start

        @block.sync
        def _(sp):
            def load_w(u, g):
                slot, src = g % 2, w[GROUPS * u + g]
                for half in range(2):
                    sp.dma_start(w_raw[64 * half:64 * half + 64, slot, :], src).then_inc(w_in[slot], 16)

            def load_x(tile, u, k):
                field = 2 * u + k if k < 2 else 2 * (CHUNKS - 1) + (k - 2) - 2 * u
                for half in range(2):
                    sp.dma_start(x_raw[64 * half:64 * half + 64, k % 2, :],
                                 xT[bass.ds(field * DIM, DIM), tile * TILE:(tile + 1) * TILE]
                                 ).then_inc(x_in[k % 2], 16)

            def load_nat(tile, c):
                sp.dma_start(x_nat[:, c, :], x_chunks[:, c, tile * TILE:(tile + 1) * TILE]
                             ).then_inc(nat_in[c], 16)

            def loads(tile, u, nat=()):
                rnd = tile * ROUNDS + u
                ends = isinstance(u, int) and u == ROUNDS - 1
                then = (tile + 1, 0) if ends else (tile, u + 1)
                for g in range(GROUPS):
                    if not (isinstance(rnd, int) and GROUPS * rnd + g < 2):
                        sp.wait_ge(w_ready, GROUPS * rnd + g - 1)
                    load_w(u, g)
                    if g == 2 and nat:
                        sp.wait_ge(prod_ready, RSTEPS * rnd)
                        for nat_tile, c in nat:
                            load_nat(nat_tile, c)
                    if then[0] < TILES:
                        sp.wait_ge(x_ready, UNITS * (rnd + 1) + g - 1 - FIRST_UNITS)
                        load_x(*then, g)

            load_x(0, 0, 0)
            load_w(0, 0)
            load_x(0, 0, 1)
            for g in range(GROUPS):
                for n in range(GROUP * g, GROUP * g + GROUP):
                    load_nat(0, (n + 1) % CHUNKS)
                if g + 1 < GROUPS:
                    if g >= 1:
                        sp.wait_ge(w_ready, g)
                    load_w(0, g + 1)
                if g < 2:
                    sp.wait_ge(x_first, g + 1)
                    load_x(0, 0, 2 + g)
            for k in range(UNITS):
                sp.wait_ge(x_ready, UNITS + k - 1 - FIRST_UNITS)
                load_x(0, 1, k)
            for tile in range(TILES):
                more = tile < TILES - 1
                if tile > 0:
                    loads(tile, 0, nat=[(tile, c) for c in range(ROUNDS - 1, CHUNKS)])
                for u in range(1, ROUNDS):
                    loads(tile, u, nat=[(tile + 1, u - 1)] if more else [])

        @block.scalar
        def _(act):
            def w_high(rnd, g):
                act.wait_ge(w_in[g % 2], 32 * (2 * rnd + g // 2 + 1))
                act.copy(w_hi[:, g % 2, :], w_raw[:, g % 2, :]).then_inc(w_hi_done, 1)

            def x_high(rnd, k):
                act.wait_ge(x_in[k % 2], 32 * (2 * rnd + k // 2 + 1))
                act.copy(x_split[:, UNITS * (rnd % 2) + k, :], x_raw[:, k % 2, :]).then_inc(x_hi, 1)

            def rows_from_psum(rnd):
                act.wait_ge(summed, BATCHES * rnd)
                for h in range(HALVES):
                    act.copy(out_rows[:, h, :], sums[:, h, :]).then_inc(rows_out, 1)

            def store_rows(rnd):
                act.wait_ge(rows_out, HALVES * rnd)
                for c in range(4):
                    act.dma_start(out[rnd - 1, 16 * c:16 * c + 16, :, :],
                                  out_rows[32 * c:32 * c + 16, :, :]).then_inc(stored, 16)

            def split(rnd, more=True):
                act.wait_ge(left_ready, RSTEPS * rnd - 8)
                w_high(rnd, 0)
                act.wait_ge(left_ready, RSTEPS * rnd)
                w_high(rnd, 1)
                if more:
                    x_high(rnd + 1, 0)
                rows_from_psum(rnd)
                act.wait_ge(left_ready, RSTEPS * rnd + 8)
                w_high(rnd, 2)
                store_rows(rnd)
                if more:
                    x_high(rnd + 1, 1)
                    x_high(rnd + 1, 2)
                act.wait_ge(left_ready, RSTEPS * rnd + 16)
                w_high(rnd, 3)
                if more:
                    x_high(rnd + 1, 3)
                act.wait_ge(stored, 64 * rnd)

            x_high(0, 0)
            w_high(0, 0)
            x_high(0, 1)
            w_high(0, 1)
            x_high(0, 2)
            x_high(0, 3)
            for g in (2, 3):
                act.wait_ge(left_ready, 8 * (g - 1))
                w_high(0, g)
            for k in range(UNITS):
                x_high(1, k)
            with act.Fori(1, ALL_ROUNDS - 1) as rnd:
                split(rnd)
            split(ALL_ROUNDS - 1, more=False)
            rows_from_psum(ALL_ROUNDS)
            store_rows(ALL_ROUNDS)
            act.wait_ge(stored, 64 * ALL_ROUNDS)

        @block.gpsimd
        def _(pool):
            def w_low(rnd, g, fields=None):
                if fields is not None:
                    pool.wait_ge(x_ready, fields)
                pool.wait_ge(w_hi_done, GROUPS * rnd + g + 1)
                pool.tensor_tensor(w_lo[:, g % 2, :], w_raw[:, g % 2, :], w_hi[:, g % 2, :].bitcast(F32),
                                   ALU.subtract).then_inc(w_ready, 1)

            def x_low(rnd, k, groups=None):
                if groups is not None:
                    pool.wait_ge(w_ready, groups)
                slot = UNITS * (rnd % 2) + k
                pool.wait_ge(x_hi, UNITS * rnd + k + 1)
                pool.tensor_tensor(x_split[64:128, slot, :], x_raw[64:128, k % 2, :],
                                   x_split[64:128, slot, :].bitcast(F32), ALU.subtract).then_inc(x_ready, 1)

            def split(rnd):
                fields, groups = UNITS * (rnd + 1) - FIRST_UNITS, GROUPS * rnd
                w_low(rnd, 0, fields=fields)
                w_low(rnd, 1)
                x_low(rnd + 1, 0, groups=groups + 2)
                w_low(rnd, 2, fields=fields + 1)
                x_low(rnd + 1, 1, groups=groups + 3)
                x_low(rnd + 1, 2)
                w_low(rnd, 3, fields=fields + 3)
                x_low(rnd + 1, 3, groups=groups + 4)

            w_low(0, 0)
            w_low(0, 1)
            x_low(0, 2, groups=2)
            x_low(0, 3)
            w_low(0, 2, fields=2)
            w_low(0, 3)
            x_low(1, 0, groups=4)
            for k in range(1, UNITS):
                x_low(1, k)
            with pool.Fori(1, ALL_ROUNDS - 1) as rnd:
                split(rnd)
            w_low(ALL_ROUNDS - 1, 0, fields=UNITS * ALL_ROUNDS - FIRST_UNITS)
            for g in range(1, GROUPS):
                w_low(ALL_ROUNDS - 1, g)

        @block.vector
        def _(dve):
            dve.memset(ones[:, :], 0.0).then_inc(ones_zero, 1)
            dve.wait_ge(ones_zero, 1)
            dve.memset(ones[0:64, 30:31], 1.0)
            dve.memset(ones[64:128, 31:32], 1.0).then_inc(ones_ready, 1)
            for k in range(FIRST_UNITS):
                dve.wait_ge(x_hi, k + 1)
                dve.tensor_tensor(x_split[64:128, k, :], x_raw[64:128, k % 2, :],
                                  x_split[64:128, k, :].bitcast(F32), ALU.subtract).then_inc(x_first, 1)

            nat_cols = x_nat[:, :, :].rearrange("p (o c) b -> p o (c b)", o=1)

            def multiply(tile, u, q, k):
                rnd = tile * ROUNDS + u
                g, h = q // HALVES, q % HALVES
                n, s = GROUP * g + k, GROUP * q + k
                to, frm = prod[:, GROUP * (q % 2) + k], left[:, LEFT_BUFFER[s]]
                if n == STEPS - 1:
                    chunks = [u, CHUNKS - 1 - u]
                elif n >= STEPS // 2:
                    t = u + (n + 1)
                    chunks = [(t + second(u, n) * (2 * CHUNKS - 1 - 2 * t)) % CHUNKS]
                else:
                    chunks = [u + (n + 1)]
                starts = [c * TILE + h * COLS for c in chunks]
                starts = [set_ahead(dve, x) for x in starts]
                if isinstance(u, int) and u == 0:
                    for c in chunks:
                        dve.wait_ge(nat_in[c], 16 * (tile + 1))
                if k == 0 and not (isinstance(rnd, int) and rnd == 0 and q < 2):
                    dve.wait_ge(summed, BATCHES * rnd + q - 1)
                dve.wait_ge(left_ready, RSTEPS * rnd + s + 1)
                for b, start in enumerate(starts):
                    blocks = slice(0, 2) if len(starts) == 1 else slice(b, b + 1)
                    x_c = nat_cols[:, :, bass.ds(start, COLS)]
                    if len(starts) == 1:
                        x_c = x_c.broadcast_to((P, 2, COLS))
                    last = dve.tensor_tensor(to[:, blocks, :], frm[:, blocks, :], x_c, ALU.mult)
                last.then_inc(prod_ready, 1)

            def whole_round(tile, u):
                for q in range(BATCHES):
                    for k in range(GROUP):
                        multiply(tile, u, q, k)

            for tile in range(TILES):
                whole_round(tile, 0)
                with dve.Fori(1, ROUNDS) as u:
                    whole_round(tile, u)

        @block.tensor
        def _(pe):
            x_cols = x_split[:, :, :].rearrange("p u b -> p (u b)")

            def product(rnd, odd, u, s, first=False):
                q, k = s // GROUP, s % GROUP
                g, h = q // HALVES, q % HALVES
                n = GROUP * g + k
                units = [UNITS * odd + (1 + 2 * b if n == STEPS - 1 else 2 * second(u, n) + b)
                         for b in range(2)]
                starts = [unit * TILE + h * COLS for unit in units]
                starts = [set_ahead(pe, x) for x in starts]
                if k == 0 and h == 0:
                    pe.wait_ge(w_ready, GROUPS * rnd + g + 1)
                if first and s == 0:
                    pe.wait_ge(x_first, FIRST_UNITS)
                elif s == 0:
                    pe.wait_ge(x_ready, UNITS * rnd + 2 - FIRST_UNITS)
                if n == STEPS // 2 and h == 0:
                    pe.wait_ge(x_ready, UNITS * (rnd + 1) - FIRST_UNITS)
                if not (first and s < BUFFERS):
                    pe.wait_ge(prod_ready, RSTEPS * rnd + s - LEFT_AGE[s] + 1)
                for b in range(2):
                    slot, col = g % 2, (2 * k + b) * P
                    to, x_i = left[:, LEFT_BUFFER[s], b, :], x_cols[:, bass.ds(starts[b], COLS)]
                    pe.matmul(to, w_hi[:, slot, col:col + P], x_i, start=True, stop=False)
                    last = pe.matmul(to, w_lo[:, slot, col:col + P], x_i, start=False, stop=True)
                last.then_inc(left_ready, 1)

            def reduce(rnd, q, first=False):
                pe.wait_ge(prod_ready, RSTEPS * rnd + GROUP * (q + 1))
                if q < HALVES and not first:
                    pe.wait_ge(rows_out, HALVES * (rnd - 1) + q + 1)
                for j in range(2 * GROUP):
                    row, m = 32 * (j % 4), 2 * (q // HALVES) + j // 4
                    last = pe.matmul(sums[row:row + 32, q % HALVES, :], ones[:, 30 - 2 * m:62 - 2 * m],
                                     prod[:, GROUP * (q % 2) + j // 2, j % 2, :],
                                     start=(m == 0), stop=(m == 2 * GROUPS - 1))
                last.then_inc(summed, 1)

            def whole_round(rnd, odd, u, first=False, final=False):
                for q in range(BATCHES):
                    for s in range(GROUP * q + LEAD, GROUP * (q + 1) + LEAD):
                        if s < RSTEPS:
                            product(rnd, odd, u, s, first)
                        elif not final:
                            product(rnd + 1, 1 - odd, 0, s - RSTEPS)
                    reduce(rnd, q, first)

            pe.wait_ge(ones_ready, 1)
            for s in range(LEAD):
                product(0, 0, 0, s, first=True)
            whole_round(0, 0, 0, first=True)
            with pe.Fori(1, ALL_ROUNDS - 1, 2) as rnd:
                u = pe.snap(rnd % ROUNDS)
                whole_round(rnd, 1, u)
                u = pe.snap((rnd + 1) % ROUNDS)
                whole_round(rnd + 1, 0, u)
            whole_round(ALL_ROUNDS - 1, 1, ROUNDS - 1, final=True)


def kernel(r_x, L0_rec_W):
    import concourse.bacc as bacc
    from concourse.bass_utils import run_bass_kernel_spmd

    x = np.asarray(r_x)
    W = np.asarray(L0_rec_W)
    xT = np.ascontiguousarray(x.transpose(1, 2, 0).reshape(FIELDS * DIM, BATCH))

    pair_of = {(int(i), int(j)): p for p, (i, j) in enumerate(zip(*np.triu_indices(FIELDS, k=1)))}
    w = np.zeros((ROUNDS, GROUPS, DIM, 2 * GROUP, 2, DIM), W.dtype)
    place = np.zeros(PAIRS, np.int64)
    for r in range(ROUNDS):
        for k, (i, js) in enumerate(round_blocks(r)):
            for h, j in enumerate(js):
                p = pair_of[min(i, j), max(i, j)]
                w[r, k // (2 * GROUP), :, k % (2 * GROUP), h, :] = W[p] if i < j else W[p].T
                place[p] = r * OUT_ROWS + 16 * (k % 4) + 2 * (k // 4) + h
    w = w.reshape(ROUNDS * GROUPS, DIM, GCOLS)

    nc = bacc.Bacc("TRN2", target_bir_lowering=False, num_devices=1)
    xT_dram = nc.dram_tensor("xT_dram", xT.shape, F32, kind="ExternalInput").ap()
    w_dram = nc.dram_tensor("w_dram", w.shape, F32, kind="ExternalInput").ap()
    out_dram = nc.dram_tensor("out_dram", (ALL_ROUNDS, OUT_ROWS, HALVES, COLS), F32, kind="ExternalOutput").ap()
    bilinear_kernel(nc, xT_dram, w_dram, out_dram)
    r = run_bass_kernel_spmd(nc, [{"xT_dram": xT, "w_dram": w}], core_ids=[0])
    got = np.asarray(r.results[0]["out_dram"]).reshape(TILES, ROUNDS * OUT_ROWS, TILE)
    return np.ascontiguousarray(got[:, place, :].transpose(0, 2, 1).reshape(BATCH, PAIRS))
```

```python
from contextlib import ExitStack

import numpy as np

import concourse.bass as bass
from concourse import mybir

F32 = mybir.dt.float32
F32R = mybir.dt.float32r
ALU = mybir.AluOpType

BATCH, FIELDS, DIM = 2048, 32, 64
PAIRS = FIELDS * (FIELDS - 1) // 2
P = 128
COLS = 512
HALVES = 2
TILE = HALVES * COLS
TILES = BATCH // TILE
QUAD = 4
QUADS = FIELDS // QUAD
ROUNDS = QUADS // 2
GROUPS = 8
PLAIN = GROUPS - 1
MIDDLE = GROUPS // 2
GROUP = 4
GCOLS = GROUP * 2 * P
GSTEPS = GROUP * HALVES
RSTEPS = GROUPS * GSTEPS
BATCHES = GROUPS * HALVES
ADDS = PLAIN * GROUP
ALL_ROUNDS = TILES * ROUNDS
SETS = 3
B_SET = 2
RING = 2 * GROUP
BUFFERS = 3
HALF_E = DIM // 2
QUAD_EVENTS = ((1, 0), (2, 1))
NEXT_EVENTS = ((4, 0), (6, 1))


def left_buffers():
    turn = [0] + [-1 if s in (1, 2) else 1 for s in range(1, RSTEPS)]
    buffers = [sum(turn[:s + 1]) % BUFFERS for s in range(RSTEPS)]
    ages = [next(d for d in range(1, RSTEPS) if buffers[s - d] == buffers[s]) for s in range(RSTEPS)]
    return buffers, ages


LEFT_BUFFER, LEFT_AGE = left_buffers()


def group_blocks(u, m):
    t = u + m + 1
    if m < PLAIN:
        q, r = (u, t) if t < QUADS else (QUADS - 1 - u, 2 * QUADS - 1 - t)
        return [(QUAD * q + k, [(QUAD * r + jj, HALF_E * b, HALF_E) for jj in range(QUAD)], 32 * k + QUAD * m)
                for k in range(GROUP) for b in range(2)]
    blocks = []
    for q in (u, QUADS - 1 - u):
        f = QUAD * q
        blocks += [(f, [f + 2, f + 3]), (f + 1, [f + 2, f + 3]), (f + 1, [f]), (f + 3, [f + 2])]
    return [(i, [(j, 0, DIM) for j in js], 32 * (n % 4) + QUAD * PLAIN + 2 * (n // 4))
            for n, (i, js) in enumerate(blocks)]


def bilinear_kernel(nc, x_fields, x_quads, w, out):
    x_chunks = x_fields.rearrange("(c p) b -> p c b", p=P)

    with ExitStack() as ctx:
        def sb(name, shape, dt=F32):
            return ctx.enter_context(nc.sbuf_tensor(name, shape, dt))

        def sem(name):
            return ctx.enter_context(nc.semaphore(name))

        x_quad = sb("x_quad", [P, 2, QUADS - 1, TILE])
        x_nat = sb("x_nat", [P, 2, SETS, TILE])
        x_hi = sb("x_hi", [P, 2, TILE], F32R)
        x_lo = sb("x_lo", [P, 2, TILE], F32R)
        x_split = sb("x_split", [P, QUAD, SETS, TILE], F32R)
        w_raw = sb("w_raw", [P, 2, GCOLS])
        w_hi = sb("w_hi", [P, 2, GCOLS], F32R)
        w_lo = sb("w_lo", [P, 2, GCOLS], F32R)
        prod = sb("prod", [P, RING, 2, COLS])
        out_rows = sb("out_rows", [P, HALVES, COLS])
        quad_ones = sb("quad_ones", [P, 60])
        plain_ones = sb("plain_ones", [P, 34])
        left = ctx.enter_context(nc.psum_tensor("left", [P, BUFFERS, 2, COLS], F32))
        sums = ctx.enter_context(nc.psum_tensor("sums", [P, HALVES, COLS], F32))

        quad_in = [sem(f"quad_in{r}") for r in range(QUADS)]
        a_in = [sem(f"a_in{c}") for c in range(2)]
        b_in = [sem(f"b_in{c}") for c in range(2)]
        w_in = [sem(f"w_in{k}") for k in range(2)]
        ones_zero = sem("ones_zero")
        ones_ready = sem("ones_ready")
        hi_done = sem("hi_done")
        lo_first = sem("lo_first")
        lo_done = sem("lo_done")
        x_copied = [sem(f"x_copied{k}") for k in range(2)]
        w_hi_done = sem("w_hi_done")
        w_ready = sem("w_ready")
        left_ready = sem("left_ready")
        prod_ready = sem("prod_ready")
        added = sem("added")
        summed = sem("summed")
        rows_out = sem("rows_out")
        stored = sem("stored")

        block = ctx.enter_context(nc.Block())


        def second(u, m):
            return (u + (m + 1)) // QUADS if m >= MIDDLE else 0

        def set_ahead(engine, start):
            if not isinstance(start, int):
                engine.compute_val(start * 4)
            return start

        @block.sync
        def _(sp):
            def load_w(number, u, m):
                if number >= 2:
                    sp.wait_ge(w_ready, number - 1)
                for half in range(2):
                    sp.dma_start(w_raw[64 * half:64 * half + 64, m % 2, :], w[GROUPS * u + m]
                                 ).then_inc(w_in[m % 2], 16)

            def load_quad(tile, r):
                sp.dma_start(x_quad[:, :, r - 1, :], x_quads[r, :, :, tile * TILE:(tile + 1) * TILE]
                             ).then_inc(quad_in[r], 16)

            def load_nat(rnd, b_quad, c):
                tile, u = rnd // ROUNDS, rnd % ROUNDS
                chunk = 2 * (QUADS - 1 - u if b_quad else u) + c
                sp.dma_start(x_nat[:, c, B_SET if b_quad else rnd % 2, :],
                             x_chunks[:, chunk, tile * TILE:(tile + 1) * TILE]
                             ).then_inc((b_in if b_quad else a_in)[c], 16)

            def copy_split(rnd, b_quad, c):
                number = 4 * rnd + 2 * b_quad + c
                to = x_split[:, :, B_SET if b_quad else rnd % 2, :].bitcast(F32)
                sp.wait_ge(hi_done, number + 1)
                for f in range(2):
                    sp.dma_start(to[0:64, 2 * c + f, :], x_hi[64 * f:64 * f + 64, c, :].bitcast(F32)
                                 ).then_inc(x_copied[c], 16)
                if number < 2:
                    sp.wait_ge(lo_first, number + 1)
                else:
                    sp.wait_ge(lo_done, number - 1)
                for f in range(2):
                    sp.dma_start(to[64:128, 2 * c + f, :], x_lo[64 * f:64 * f + 64, c, :].bitcast(F32)
                                 ).then_inc(x_copied[c], 16)

            for rnd in range(ALL_ROUNDS):
                tile, u = rnd // ROUNDS, rnd % ROUNDS
                more = rnd + 1 < ALL_ROUNDS
                if rnd == 0:
                    load_nat(0, False, 0)
                    load_w(0, 0, 0)
                    load_nat(0, False, 1)
                    copy_split(0, False, 0)
                    load_quad(0, 1)
                    copy_split(0, False, 1)
                    load_w(1, 0, 1)
                    load_quad(0, 2)
                for m in range(GROUPS):
                    ahead = GROUPS * rnd + m + 2
                    if ahead < GROUPS * ALL_ROUNDS:
                        load_w(ahead, ahead // GROUPS % ROUNDS, ahead % GROUPS)
                    if m == 0:
                        if rnd > 0:
                            sp.wait_ge(prod_ready, RSTEPS * rnd)
                        for c in range(2):
                            load_nat(rnd, True, c)
                        if u > 0 and tile + 1 < TILES:
                            load_quad(tile + 1, u)
                    if m == 2 and more:
                        for c in range(2):
                            load_nat(rnd + 1, False, c)
                    if rnd == 0 and m + 3 < QUADS:
                        load_quad(0, m + 3)
                    if rnd > 0 and u == 0 and m + ROUNDS < QUADS:
                        load_quad(tile, m + ROUNDS)
                    for at, c in QUAD_EVENTS:
                        if at == m:
                            copy_split(rnd, True, c)
                    for at, c in NEXT_EVENTS:
                        if at == m and more:
                            copy_split(rnd + 1, False, c)

        @block.scalar
        def _(act):
            def w_high(rnd, m):
                act.wait_ge(w_in[m % 2], 32 * (GROUPS // 2 * rnd + m // 2 + 1))
                act.copy(w_hi[:, m % 2, :], w_raw[:, m % 2, :]).then_inc(w_hi_done, 1)

            def x_high(rnd, b_quad, c, first=False):
                act.wait_ge((b_in if b_quad else a_in)[c], 16 * (rnd + 1))
                if not first:
                    act.wait_ge(x_copied[c], 64 * (2 * rnd + b_quad))
                act.copy(x_hi[:, c, :], x_nat[:, c, B_SET if b_quad else rnd % 2, :]).then_inc(hi_done, 1)

            def rows_from_psum(rnd):
                for h in range(HALVES):
                    act.wait_ge(summed, BATCHES * rnd - (1 - h))
                    act.copy(out_rows[:, h, :], sums[:, h, :]).then_inc(rows_out, 1)

            def store_rows(rnd):
                act.wait_ge(rows_out, HALVES * rnd)
                act.dma_start(out[rnd - 1], out_rows[:, :, :]).then_inc(stored, 16)

            def split(rnd, first=False, final=False):
                for m in range(GROUPS):
                    if not (final and m == GROUPS - 1):
                        if not (first and m == 0):
                            act.wait_ge(left_ready, RSTEPS * rnd + GSTEPS * m)
                        if m + 1 < GROUPS:
                            w_high(rnd, m + 1)
                        else:
                            w_high(rnd + 1, 0)
                    if m == 0 and not first:
                        rows_from_psum(rnd)
                    if m == 1 and not first:
                        store_rows(rnd)
                    if m == 4 and not first:
                        act.wait_ge(stored, 16 * rnd)
                    for at, c in QUAD_EVENTS:
                        if at == m:
                            x_high(rnd, True, c)
                    for at, c in NEXT_EVENTS:
                        if at == m and not final:
                            x_high(rnd + 1, False, c)

            x_high(0, False, 0, first=True)
            w_high(0, 0)
            x_high(0, False, 1, first=True)
            split(0, first=True)
            with act.Fori(1, ALL_ROUNDS - 1) as rnd:
                split(rnd)
            split(ALL_ROUNDS - 1, final=True)
            rows_from_psum(ALL_ROUNDS)
            store_rows(ALL_ROUNDS)
            act.wait_ge(stored, 16 * ALL_ROUNDS)

        @block.gpsimd
        def _(pool):
            def w_low(rnd, m):
                pool.wait_ge(w_hi_done, GROUPS * rnd + m + 1)
                pool.tensor_tensor(w_lo[:, m % 2, :], w_raw[:, m % 2, :], w_hi[:, m % 2, :].bitcast(F32),
                                   ALU.subtract).then_inc(w_ready, 1)

            def x_low(rnd, b_quad, c):
                pool.wait_ge(hi_done, 4 * rnd + 2 * b_quad + c + 1)
                pool.tensor_tensor(x_lo[:, c, :], x_nat[:, c, B_SET if b_quad else rnd % 2, :],
                                   x_hi[:, c, :].bitcast(F32), ALU.subtract).then_inc(lo_done, 1)

            def add_halves(rnd, m):
                for k in range(GROUP):
                    pool.wait_ge(prod_ready, RSTEPS * rnd + GSTEPS * m + k + 1)
                    pool.tensor_tensor(prod[:, k, 0, :], prod[:, k, 0, :], prod[:, k, 1, :],
                                       ALU.add).then_inc(added, 1)

            def whole_round(rnd, final=False):
                for m in range(GROUPS):
                    if m + 1 < GROUPS:
                        w_low(rnd, m + 1)
                        add_halves(rnd, m)
                    elif not final:
                        w_low(rnd + 1, 0)
                    for at, c in QUAD_EVENTS:
                        if at == m:
                            x_low(rnd, True, c)
                    for at, c in NEXT_EVENTS:
                        if at == m and not final:
                            x_low(rnd + 1, False, c)

            w_low(0, 0)
            with pool.Fori(0, ALL_ROUNDS - 1) as rnd:
                whole_round(rnd)
            whole_round(ALL_ROUNDS - 1, final=True)

        @block.vector
        def _(dve):
            dve.memset(quad_ones[:, :], 0.0)
            dve.memset(plain_ones[:, :], 0.0).then_inc(ones_zero, 1)
            dve.wait_ge(ones_zero, 1)
            for j in range(QUAD):
                dve.memset(quad_ones[32 * j:32 * j + 32, 28 + j:29 + j], 1.0)
            dve.memset(plain_ones[0:64, 30:31], 1.0)
            dve.memset(plain_ones[64:128, 31:32], 1.0).then_inc(ones_ready, 1)
            for c in range(2):
                dve.wait_ge(hi_done, c + 1)
                dve.tensor_tensor(x_lo[:, c, :], x_nat[:, c, 0, :], x_hi[:, c, :].bitcast(F32),
                                  ALU.subtract).then_inc(lo_first, 1)

            quad_cols = x_quad[:, :, :, :].rearrange("p e r b -> p e (r b)")
            nat_cols = x_nat[:, :, :, :].rearrange("p c s b -> p c (s b)")

            def multiply(tile, u, m, h, k):
                rnd = tile * ROUNDS + u
                s = GSTEPS * m + GROUP * h + k
                if m < PLAIN:
                    t = u + (m + 1)
                    r = t
                    if m >= MIDDLE:
                        r = t + second(u, m) * (2 * QUADS - 1 - 2 * t)
                    start = set_ahead(dve, (r - 1) % (QUADS - 1) * TILE)
                    x_j = quad_cols[:, :, h * COLS:][:, :, bass.ds(start, COLS)]
                else:
                    start = set_ahead(dve, (rnd % 2 if k < 2 else B_SET) * TILE)
                    at_h = nat_cols[:, :, h * COLS:]
                    if k % 2 == 0:
                        x_j = at_h[:, 1:2, bass.ds(start, COLS)].broadcast_to((P, 2, COLS))
                    else:
                        x_j = at_h[:, :, bass.ds(start, COLS)]
                if k == 0:
                    if isinstance(u, int) and u == 0 and m < PLAIN and h == 0:
                        dve.wait_ge(quad_in[m + 1], 16 * (tile + 1))
                    if not (isinstance(rnd, int) and rnd == 0 and m == 0):
                        dve.wait_ge(summed, BATCHES * rnd + 2 * m - 1 + h)
                dve.wait_ge(left_ready, RSTEPS * rnd + s + 1)
                dve.tensor_tensor(prod[:, GROUP * h + k, :, :], left[:, LEFT_BUFFER[s]], x_j,
                                  ALU.mult).then_inc(prod_ready, 1)

            def whole_round(tile, u):
                for m in range(GROUPS):
                    for h in range(HALVES):
                        for k in range(GROUP):
                            multiply(tile, u, m, h, k)

            for tile in range(TILES):
                whole_round(tile, 0)
                with dve.Fori(1, ROUNDS) as u:
                    whole_round(tile, u)

        @block.tensor
        def _(pe):
            x_cols = x_split[:, :, :, :].rearrange("p f s b -> p f (s b)")

            def product(rnd, odd, u, s, first=False):
                m, h, k = s // GSTEPS, s // GROUP % HALVES, s % GROUP
                if m < PLAIN:
                    fields = [k, k]
                    start = set_ahead(pe, (odd + second(u, m) * (B_SET - odd)) * TILE)
                else:
                    fields = [0, 1] if k % 2 == 0 else [1, 3]
                    start = (odd if k < 2 else B_SET) * TILE
                if k == 0 and h == 0:
                    pe.wait_ge(w_ready, GROUPS * rnd + m + 1)
                if m == 0 and h == 0 and k % 2 == 0:
                    pe.wait_ge(x_copied[k // 2], 64 * (2 * rnd + 1))
                if m == MIDDLE and h == 0 and k % 2 == 0:
                    pe.wait_ge(x_copied[k // 2], 64 * (2 * rnd + 2))
                if not (first and s < BUFFERS):
                    pe.wait_ge(prod_ready, RSTEPS * rnd + s - LEFT_AGE[s] + 1)
                for b in range(2):
                    col = (2 * k + b) * P
                    to = left[:, LEFT_BUFFER[s], b, :]
                    x_i = x_cols[:, fields[b], h * COLS:][:, bass.ds(start, COLS)]
                    pe.matmul(to, w_hi[:, m % 2, col:col + P], x_i, start=True, stop=False)
                    last = pe.matmul(to, w_lo[:, m % 2, col:col + P], x_i, start=False, stop=True)
                last.then_inc(left_ready, 1)

            def reduce(rnd, m, h, first=False):
                if h == 0 and m < PLAIN:
                    pe.wait_ge(added, ADDS * rnd + GROUP * (m + 1))
                    blocks = [(k, 0) for k in range(GROUP)]
                else:
                    pe.wait_ge(prod_ready, RSTEPS * rnd + GSTEPS * m + GROUP * (h + 1))
                    blocks = [(k, b) for b in range(2) for k in range(GROUP)]
                if m == 0 and not first:
                    pe.wait_ge(rows_out, HALVES * (rnd - 1) + h + 1)
                if m == PLAIN:
                    blocks = [(n // 2, n % 2) for n in range(2 * GROUP)]
                for n, (k, b) in enumerate(blocks):
                    if m < PLAIN:
                        selector = quad_ones[:, 28 - QUAD * m:60 - QUAD * m]
                    else:
                        selector = plain_ones[:, 2 - 2 * (n // 4):34 - 2 * (n // 4)]
                    row = 32 * (n % 4)
                    last = pe.matmul(sums[row:row + 32, h, :], selector, prod[:, GROUP * h + k, b, :],
                                     start=(m == 0 and n < 4), stop=(m == PLAIN and n >= 4))
                last.then_inc(summed, 1)

            def whole_round(rnd, odd, u, first=False, final=False):
                def following(s):
                    if s < RSTEPS:
                        product(rnd, odd, u, s, first)
                    elif not final:
                        product(rnd + 1, 1 - odd, 0, s - RSTEPS)

                for m in range(GROUPS):
                    for s in range(3, 8):
                        following(GSTEPS * m + s)
                    reduce(rnd, m, 0, first)
                    for s in range(8, 11):
                        following(GSTEPS * m + s)
                    reduce(rnd, m, 1, first)

            pe.wait_ge(ones_ready, 1)
            for s in range(3):
                product(0, 0, 0, s, first=True)
            whole_round(0, 0, 0, first=True)
            with pe.Fori(1, ALL_ROUNDS - 1, 2) as rnd:
                u = pe.snap(rnd % ROUNDS)
                whole_round(rnd, 1, u)
                u = pe.snap((rnd + 1) % ROUNDS)
                whole_round(rnd + 1, 0, u)
            whole_round(ALL_ROUNDS - 1, 1, ROUNDS - 1, final=True)


def kernel(r_x, L0_rec_W):
    import concourse.bacc as bacc
    from concourse.bass_utils import run_bass_kernel_spmd

    x = np.asarray(r_x)
    W = np.asarray(L0_rec_W)
    xT = np.ascontiguousarray(x.transpose(1, 2, 0))
    x_quads = np.ascontiguousarray(
        xT.reshape(QUADS, QUAD, 2, HALF_E, BATCH).transpose(0, 1, 3, 2, 4).reshape(QUADS, P, 2, BATCH))
    xT = xT.reshape(FIELDS * DIM, BATCH)

    pair_of = {(int(i), int(j)): p for p, (i, j) in enumerate(zip(*np.triu_indices(FIELDS, k=1)))}
    w = np.zeros((ROUNDS, GROUPS, DIM, 2 * GROUP, P), W.dtype)
    place = np.zeros(PAIRS, np.int64)
    for u in range(ROUNDS):
        for m in range(GROUPS):
            for n, (i, js, row) in enumerate(group_blocks(u, m)):
                for a, (j, e, size) in enumerate(js):
                    p = pair_of[min(i, j), max(i, j)]
                    w_ij = W[p] if i < j else W[p].T
                    w[u, m, :, n, size * a:size * (a + 1)] = w_ij[:, e:e + size]
                    place[p] = P * u + row + a
    w = w.reshape(ROUNDS * GROUPS, DIM, GCOLS)

    nc = bacc.Bacc("TRN2", target_bir_lowering=False, num_devices=1)
    xT_dram = nc.dram_tensor("xT_dram", xT.shape, F32, kind="ExternalInput").ap()
    xq_dram = nc.dram_tensor("xq_dram", x_quads.shape, F32, kind="ExternalInput").ap()
    w_dram = nc.dram_tensor("w_dram", w.shape, F32, kind="ExternalInput").ap()
    out_dram = nc.dram_tensor("out_dram", (ALL_ROUNDS, P, HALVES, COLS), F32, kind="ExternalOutput").ap()
    bilinear_kernel(nc, xT_dram, xq_dram, w_dram, out_dram)
    r = run_bass_kernel_spmd(nc, [{"xT_dram": xT, "xq_dram": x_quads, "w_dram": w}], core_ids=[0])
    got = np.asarray(r.results[0]["out_dram"]).reshape(TILES, ROUNDS * P, TILE)
    return np.ascontiguousarray(got[:, place, :].transpose(0, 2, 1).reshape(BATCH, PAIRS))
```

```python
from contextlib import ExitStack

import numpy as np

import concourse.bass as bass
from concourse import mybir

F32 = mybir.dt.float32
F32R = mybir.dt.float32r
ALU = mybir.AluOpType

BATCH, FIELDS, DIM = 2048, 32, 64
PAIRS = FIELDS * (FIELDS - 1) // 2
P = 128
COLS = 512
HALVES = 2
TILE = HALVES * COLS
TILES = BATCH // TILE
QUAD = 4
QUADS = FIELDS // QUAD
ROUNDS = QUADS // 2
GROUPS = 8
PLAIN = GROUPS - 1
MIDDLE = GROUPS // 2
GROUP = 4
GCOLS = GROUP * 2 * P
GSTEPS = GROUP * HALVES
RSTEPS = GROUPS * GSTEPS
BATCHES = GROUPS * HALVES
ALL_ROUNDS = TILES * ROUNDS
SETS = 3
B_SET = 2
RING = 2 * GROUP
BUFFERS = 3
WARM = 4
HALF_E = DIM // 2
B_SPLITS = ((1, 0), (2, 1))
NEXT_SPLITS = ((6, 0), (7, 1))
ADD_COLS = (160, 0, 0, 160, 160, 160, 0, 0)


def left_buffers():
    turn = [0] + [-1 if s in (1, 2) else 1 for s in range(1, RSTEPS)]
    buffers = [sum(turn[:s + 1]) % BUFFERS for s in range(RSTEPS)]
    ages = [next(d for d in range(1, RSTEPS) if buffers[s - d] == buffers[s]) for s in range(RSTEPS)]
    return buffers, ages


LEFT_BUFFER, LEFT_AGE = left_buffers()


def adds_until(m, h):
    return GROUP * sum(1 + (ADD_COLS[g] > 0 and (g < m or h == 1)) for g in range(min(m + 1, PLAIN)))


ADDS = adds_until(PLAIN, 1)


def group_blocks(u, m):
    t = u + m + 1
    if m < PLAIN:
        q, r = (u, t) if t < QUADS else (QUADS - 1 - u, 2 * QUADS - 1 - t)
        return [(QUAD * q + k, [(QUAD * r + jj, HALF_E * b, HALF_E) for jj in range(QUAD)], 32 * k + QUAD * m)
                for k in range(GROUP) for b in range(2)]
    blocks = []
    for q in (u, QUADS - 1 - u):
        f = QUAD * q
        blocks += [(f, [f + 2, f + 3]), (f + 1, [f + 2, f + 3]), (f + 1, [f]), (f + 3, [f + 2])]
    return [(i, [(j, 0, DIM) for j in js], 32 * (n % 4) + QUAD * PLAIN + 2 * (n // 4))
            for n, (i, js) in enumerate(blocks)]


def bilinear_kernel(nc, x_fields, x_quads, w, out):
    x_chunks = x_fields.rearrange("(c p) b -> p c b", p=P)
    x_rows = x_fields.rearrange("(f d) b -> d f b", d=DIM)

    with ExitStack() as ctx:
        def sb(name, shape, dt=F32):
            return ctx.enter_context(nc.sbuf_tensor(name, shape, dt))

        def sem(name):
            return ctx.enter_context(nc.semaphore(name))

        x_quad = sb("x_quad", [P, 2, QUADS - 1, TILE])
        x_nat = sb("x_nat", [P, 2, SETS, TILE])
        x_hi = sb("x_hi", [P, 2, TILE], F32R)
        x_lo = sb("x_lo", [P, 2, TILE], F32R)
        x_split = sb("x_split", [P, QUAD, SETS, TILE], F32R)
        w_raw = sb("w_raw", [P, 2, GCOLS])
        w_hi = sb("w_hi", [P, 2, GCOLS], F32R)
        w_lo = sb("w_lo", [P, 2, GCOLS], F32R)
        prod = sb("prod", [P, RING, 2, COLS])
        out_rows = sb("out_rows", [P, HALVES, COLS])
        quad_ones = sb("quad_ones", [P, 60])
        plain_ones = sb("plain_ones", [P, 34])
        left = ctx.enter_context(nc.psum_tensor("left", [P, BUFFERS, 2, COLS], F32))
        sums = ctx.enter_context(nc.psum_tensor("sums", [P, HALVES, COLS], F32))

        first_in = [sem(f"first_in{n}") for n in range(4)]
        first_hi = sem("first_hi")
        first_lo = sem("first_lo")
        quad_in = [sem(f"quad_in{r}") for r in range(QUADS)]
        quad_late = sem("quad_late")
        a_in = [sem(f"a_in{c}") for c in range(2)]
        b_in = [sem(f"b_in{c}") for c in range(2)]
        w_in = [sem(f"w_in{k}") for k in range(2)]
        ones_zero = sem("ones_zero")
        ones_ready = sem("ones_ready")
        hi_done = sem("hi_done")
        lo_done = sem("lo_done")
        x_copied = [sem(f"x_copied{k}") for k in range(2)]
        w_hi_done = sem("w_hi_done")
        w_ready = sem("w_ready")
        left_ready = sem("left_ready")
        prod_ready = sem("prod_ready")
        added = sem("added")
        summed = sem("summed")
        rows_out = sem("rows_out")
        stored = sem("stored")

        block = ctx.enter_context(nc.Block())


        def second(u, m):
            return (u + (m + 1)) // QUADS if m >= MIDDLE else 0

        def set_ahead(engine, start):
            if not isinstance(start, int):
                engine.compute_val(start * 4)
            return start

        @block.sync
        def _(sp):
            def load_w(number, u, m):
                if number >= 2:
                    sp.wait_ge(w_ready, 2 * (number - 1))
                for half in range(2):
                    sp.dma_start(w_raw[64 * half:64 * half + 64, m % 2, :], w[GROUPS * u + m]
                                 ).then_inc(w_in[m % 2], 16)

            def load_quad(tile, r):
                sp.dma_start(x_quad[:, :, r - 1, :], x_quads[r, :, :, tile * TILE:(tile + 1) * TILE]
                             ).then_inc(quad_in[r], 16)

            def load_quad_half(h):
                at = slice(h * COLS, (h + 1) * COLS)
                sp.dma_start(x_quad[:, :, 0, at], x_quads[1, :, :, at]).then_inc(quad_late if h else quad_in[1], 16)

            def load_first(n):
                c, h = n % 2, n // 2
                for half in range(2):
                    sp.dma_start(prod[64 * half:64 * half + 64, GROUP + n, :, :],
                                 x_rows[:, 2 * c:2 * c + 2, h * COLS:(h + 1) * COLS]
                                 ).then_inc(first_in[n], 16)

            def load_nat(rnd, b_quad, c):
                tile, u = rnd // ROUNDS, rnd % ROUNDS
                chunk = 2 * (QUADS - 1 - u if b_quad else u) + c
                sp.dma_start(x_nat[:, c, B_SET if b_quad else rnd % 2, :],
                             x_chunks[:, chunk, tile * TILE:(tile + 1) * TILE]
                             ).then_inc((b_in if b_quad else a_in)[c], 16)

            def copy_split(rnd, b_quad, c):
                number = 4 * rnd - 2 * (not b_quad) + c
                to = x_split[:, :, B_SET if b_quad else rnd % 2, :].bitcast(F32)
                sp.wait_ge(hi_done, number + 1)
                for f in range(2):
                    sp.dma_start(to[0:64, 2 * c + f, :], x_hi[64 * f:64 * f + 64, c, :].bitcast(F32)
                                 ).then_inc(x_copied[c], 16)
                sp.wait_ge(lo_done, number + 1)
                for f in range(2):
                    sp.dma_start(to[64:128, 2 * c + f, :], x_lo[64 * f:64 * f + 64, c, :].bitcast(F32)
                                 ).then_inc(x_copied[c], 16)

            for rnd in range(ALL_ROUNDS):
                tile, u = rnd // ROUNDS, rnd % ROUNDS
                more = rnd + 1 < ALL_ROUNDS
                if rnd == 0:
                    load_w(0, 0, 0)
                    load_first(0)
                    load_first(1)
                    load_quad_half(0)
                    load_first(2)
                    load_first(3)
                    load_w(1, 0, 1)
                    load_quad_half(1)
                    load_quad(0, 2)
                for m in range(GROUPS):
                    ahead = GROUPS * rnd + m + 2
                    if ahead < GROUPS * ALL_ROUNDS:
                        load_w(ahead, ahead // GROUPS % ROUNDS, ahead % GROUPS)
                    if m == 0:
                        if rnd > 0:
                            sp.wait_ge(prod_ready, RSTEPS * rnd)
                        for c in range(2):
                            load_nat(rnd, True, c)
                        if u > 0 and tile + 1 < TILES:
                            load_quad(tile + 1, u)
                    if m == 1 and rnd == 0:
                        for c in range(2):
                            load_nat(0, False, c)
                    if m == 3 and more:
                        if rnd == 0:
                            for c in range(2):
                                sp.wait_ge(a_in[c], 16)
                        for c in range(2):
                            load_nat(rnd + 1, False, c)
                    if rnd == 0 and m + 3 < QUADS:
                        load_quad(0, m + 3)
                    if rnd > 0 and u == 0 and m + ROUNDS < QUADS:
                        load_quad(tile, m + ROUNDS)
                    for at, c in B_SPLITS:
                        if at == m:
                            copy_split(rnd, True, c)
                    for at, c in NEXT_SPLITS:
                        if at == m and more:
                            copy_split(rnd + 1, False, c)

        @block.scalar
        def _(act):
            def w_high(rnd, m):
                act.wait_ge(w_in[m % 2], 32 * (GROUPS // 2 * rnd + m // 2 + 1))
                act.copy(w_hi[:, m % 2, :], w_raw[:, m % 2, :]).then_inc(w_hi_done, 1)

            def first_high(n):
                c, h = n % 2, n // 2
                act.wait_ge(first_in[n], 32)
                act.copy(x_split[:, 2 * c:2 * c + 2, 0, h * COLS:(h + 1) * COLS], prod[:, GROUP + n, :, :]
                         ).then_inc(first_hi, 1)

            def x_high(rnd, b_quad, c, first=False):
                act.wait_ge((b_in if b_quad else a_in)[c], 16 * (rnd + 1))
                if not first:
                    act.wait_ge(x_copied[c], 64 * (2 * rnd - (not b_quad)))
                act.copy(x_hi[:, c, :], x_nat[:, c, B_SET if b_quad else rnd % 2, :]).then_inc(hi_done, 1)

            def copy_and_store_rows(rnd):
                for h in range(HALVES):
                    act.wait_ge(summed, BATCHES * rnd - (1 - h))
                    act.copy(out_rows[:, h, :], sums[:, h, :]).then_inc(rows_out, 1)
                    act.wait_ge(rows_out, HALVES * (rnd - 1) + h + 1)
                    act.dma_start(out[rnd - 1, :, h, :], out_rows[:, h, :]).then_inc(stored, 16)

            def split(rnd, first=False, final=False):
                for m in range(GROUPS):
                    if not (final and m == GROUPS - 1):
                        if not (first and m == 0):
                            act.wait_ge(left_ready, RSTEPS * rnd + GSTEPS * m)
                        if m + 1 < GROUPS:
                            w_high(rnd, m + 1)
                        else:
                            w_high(rnd + 1, 0)
                    if m == 0 and not first:
                        copy_and_store_rows(rnd)
                    if m == 4 and not first:
                        act.wait_ge(stored, 32 * rnd)
                    for at, c in B_SPLITS:
                        if at == m:
                            x_high(rnd, True, c, first)
                    for at, c in NEXT_SPLITS:
                        if at == m and not final:
                            x_high(rnd + 1, False, c)

            w_high(0, 0)
            for n in range(4):
                first_high(n)
            split(0, first=True)
            with act.Fori(1, ALL_ROUNDS - 1) as rnd:
                split(rnd)
            split(ALL_ROUNDS - 1, final=True)
            copy_and_store_rows(ALL_ROUNDS)
            act.wait_ge(stored, 32 * ALL_ROUNDS)

        @block.gpsimd
        def _(pool):
            def w_low(rnd, m, part):
                at = slice(part * GCOLS // 2, (part + 1) * GCOLS // 2)
                pool.wait_ge(w_hi_done, GROUPS * rnd + m + 1)
                pool.tensor_tensor(w_lo[:, m % 2, at], w_raw[:, m % 2, at], w_hi[:, m % 2, at].bitcast(F32),
                                   ALU.subtract).then_inc(w_ready, 1)

            def x_low(rnd, b_quad, c):
                pool.wait_ge(hi_done, 4 * rnd - 2 * (not b_quad) + c + 1)
                pool.tensor_tensor(x_lo[:, c, :], x_nat[:, c, B_SET if b_quad else rnd % 2, :],
                                   x_hi[:, c, :].bitcast(F32), ALU.subtract).then_inc(lo_done, 1)

            def add_halves(rnd, m, h, k):
                cols, n = ADD_COLS[m] if h else COLS, GROUP * h + k
                pool.wait_ge(prod_ready, RSTEPS * rnd + GSTEPS * m + n + 1)
                pool.tensor_tensor(prod[:, n, 0, :cols], prod[:, n, 0, :cols], prod[:, n, 1, :cols],
                                   ALU.add).then_inc(added, 1)

            def whole_round(rnd, final=False):
                for m in range(GROUPS):
                    if m < PLAIN:
                        for k in range(GROUP - 1):
                            add_halves(rnd, m, 0, k)
                        w_low(rnd, m + 1, 0)
                        add_halves(rnd, m, 0, GROUP - 1)
                        w_low(rnd, m + 1, 1)
                    elif not final:
                        w_low(rnd + 1, 0, 0)
                        w_low(rnd + 1, 0, 1)
                    if ADD_COLS[m]:
                        for k in range(GROUP):
                            add_halves(rnd, m, 1, k)
                    for at, c in B_SPLITS:
                        if at == m:
                            x_low(rnd, True, c)
                    for at, c in NEXT_SPLITS:
                        if at == m and not final:
                            x_low(rnd + 1, False, c)

            w_low(0, 0, 0)
            w_low(0, 0, 1)
            whole_round(0)
            with pool.Fori(1, ALL_ROUNDS - 1) as rnd:
                whole_round(rnd)
            whole_round(ALL_ROUNDS - 1, final=True)

        @block.vector
        def _(dve):
            dve.memset(prod[:, 0, 0, :], 0.0)
            dve.memset(quad_ones[:, :], 0.0)
            dve.memset(plain_ones[:, :], 0.0).then_inc(ones_zero, 1)
            dve.wait_ge(ones_zero, 1)
            for j in range(QUAD):
                dve.memset(quad_ones[32 * j:32 * j + 32, 28 + j:29 + j], 1.0)
            dve.memset(plain_ones[0:64, 30:31], 1.0)
            dve.memset(plain_ones[64:128, 31:32], 1.0).then_inc(ones_ready, 1)

            def first_low(n):
                c, h = n % 2, n // 2
                dve.wait_ge(first_hi, n + 1)
                piece = x_split[64:128, 2 * c:2 * c + 2, 0, h * COLS:(h + 1) * COLS]
                dve.tensor_tensor(piece, prod[64:128, GROUP + n, :, :], piece.bitcast(F32),
                                  ALU.subtract).then_inc(first_lo, 1)

            quad_cols = x_quad[:, :, :, :].rearrange("p e r b -> p e (r b)")
            nat_cols = x_nat[:, :, :, :].rearrange("p c s b -> p c (s b)")

            def multiply(tile, u, m, h, k):
                rnd = tile * ROUNDS + u
                s = GSTEPS * m + GROUP * h + k
                if m < PLAIN:
                    t = u + (m + 1)
                    r = t
                    if m >= MIDDLE:
                        r = t + second(u, m) * (2 * QUADS - 1 - 2 * t)
                    start = set_ahead(dve, (r - 1) % (QUADS - 1) * TILE)
                    x_j = quad_cols[:, :, h * COLS:][:, :, bass.ds(start, COLS)]
                else:
                    start = set_ahead(dve, (rnd % 2 if k < 2 else B_SET) * TILE)
                    at_h = nat_cols[:, :, h * COLS:]
                    if k % 2 == 0:
                        x_j = at_h[:, 1:2, bass.ds(start, COLS)].broadcast_to((P, 2, COLS))
                    else:
                        x_j = at_h[:, :, bass.ds(start, COLS)]
                if isinstance(rnd, int) and rnd == 0:
                    if m == 0 and h == 1 and k == 0:
                        dve.wait_ge(quad_late, 16)
                    if m == PLAIN and h == 0 and k < 2:
                        dve.wait_ge(a_in[1 - k], 16)
                if k == 0:
                    if isinstance(u, int) and u == 0 and m < PLAIN and h == 0:
                        dve.wait_ge(quad_in[m + 1], 16 * (tile + 1))
                    if not (isinstance(rnd, int) and rnd == 0 and m == 0):
                        dve.wait_ge(summed, BATCHES * rnd + 2 * m - 1 + h)
                dve.wait_ge(left_ready, RSTEPS * rnd + s + 1)
                dve.tensor_tensor(prod[:, GROUP * h + k, :, :], left[:, LEFT_BUFFER[s]], x_j,
                                  ALU.mult).then_inc(prod_ready, 1)

            def whole_round(tile, u):
                for m in range(GROUPS):
                    for h in range(HALVES):
                        for k in range(GROUP):
                            multiply(tile, u, m, h, k)
                            if isinstance(u, int) and tile == 0 and (m, h) == (0, 0) and k in (1, 2):
                                first_low(k + 1)

            first_low(0)
            first_low(1)
            for tile in range(TILES):
                whole_round(tile, 0)
                with dve.Fori(1, ROUNDS) as u:
                    whole_round(tile, u)

        @block.tensor
        def _(pe):
            x_cols = x_split[:, :, :, :].rearrange("p f s b -> p f (s b)")

            def product(rnd, odd, u, s, first=False):
                m, h, k = s // GSTEPS, s // GROUP % HALVES, s % GROUP
                if m < PLAIN:
                    fields = [k, k]
                    start = set_ahead(pe, (odd + second(u, m) * (B_SET - odd)) * TILE)
                else:
                    fields = [0, 1] if k % 2 == 0 else [1, 3]
                    start = (odd if k < 2 else B_SET) * TILE
                if k % 2 == 0 and h == 0:
                    pe.wait_ge(w_ready, 2 * (GROUPS * rnd + m) + k // 2 + 1)
                if m == 0 and first and k % 2 == 0:
                    pe.wait_ge(first_lo, 2 * h + k // 2 + 1)
                elif m == 0 and h == 0 and k % 2 == 0:
                    pe.wait_ge(x_copied[k // 2], 64 * 2 * rnd)
                if m == MIDDLE and h == 0 and k % 2 == 0:
                    pe.wait_ge(x_copied[k // 2], 64 * (2 * rnd + 1))
                if not (first and s < BUFFERS):
                    pe.wait_ge(prod_ready, RSTEPS * rnd + s - LEFT_AGE[s] + 1)
                for b in range(2):
                    col = (2 * k + b) * P
                    to = left[:, LEFT_BUFFER[s], b, :]
                    x_i = x_cols[:, fields[b], h * COLS:][:, bass.ds(start, COLS)]
                    pe.matmul(to, w_hi[:, m % 2, col:col + P], x_i, start=True, stop=False)
                    last = pe.matmul(to, w_lo[:, m % 2, col:col + P], x_i, start=False, stop=True)
                last.then_inc(left_ready, 1)

            def reduce(rnd, m, h, first=False):
                cols = 0 if m == PLAIN else ADD_COLS[m] if h else COLS
                if cols:
                    pe.wait_ge(added, ADDS * rnd + adds_until(m, h))
                else:
                    pe.wait_ge(prod_ready, RSTEPS * rnd + GSTEPS * m + GROUP * (h + 1))
                blocks = [(k, b) for b in range(2) for k in range(GROUP) if b == 0 or cols < COLS]
                if m == 0 and not first:
                    pe.wait_ge(rows_out, HALVES * (rnd - 1) + h + 1)
                if m == PLAIN:
                    blocks = [(n // 2, n % 2) for n in range(2 * GROUP)]
                for n, (k, b) in enumerate(blocks):
                    if m < PLAIN:
                        selector = quad_ones[:, 28 - QUAD * m:60 - QUAD * m]
                    else:
                        selector = plain_ones[:, 2 - 2 * (n // 4):34 - 2 * (n // 4)]
                    row = 32 * (n % 4)
                    at = slice(cols if m < PLAIN and b == 1 else 0, COLS)
                    last = pe.matmul(sums[row:row + 32, h, at], selector, prod[:, GROUP * h + k, b, at],
                                     start=(m == 0 and n < 4), stop=(m == PLAIN and n >= 4))
                last.then_inc(summed, 1)

            def whole_round(rnd, odd, u, first=False, final=False):
                def following(s):
                    if s < RSTEPS:
                        product(rnd, odd, u, s, first)
                    elif not final:
                        product(rnd + 1, 1 - odd, 0, s - RSTEPS)

                for m in range(GROUPS):
                    for s in range(3, 8):
                        following(GSTEPS * m + s)
                    reduce(rnd, m, 0, first)
                    for s in range(8, 11):
                        following(GSTEPS * m + s)
                    reduce(rnd, m, 1, first)

            pe.wait_ge(ones_ready, 1)
            for _ in range(WARM):
                pe.matmul(left[0:32, BUFFERS - 1, 0, :], quad_ones[:, 0:32], prod[:, 0, 0, :],
                          start=True, stop=True)
            for s in range(3):
                product(0, 0, 0, s, first=True)
            whole_round(0, 0, 0, first=True)
            with pe.Fori(1, ALL_ROUNDS - 1, 2) as rnd:
                u = pe.snap(rnd % ROUNDS)
                whole_round(rnd, 1, u)
                u = pe.snap((rnd + 1) % ROUNDS)
                whole_round(rnd + 1, 0, u)
            whole_round(ALL_ROUNDS - 1, 1, ROUNDS - 1, final=True)


def kernel(r_x, L0_rec_W):
    import concourse.bacc as bacc
    from concourse.bass_utils import run_bass_kernel_spmd

    x = np.asarray(r_x)
    W = np.asarray(L0_rec_W)
    xT = np.ascontiguousarray(x.transpose(1, 2, 0))
    x_quads = np.ascontiguousarray(
        xT.reshape(QUADS, QUAD, 2, HALF_E, BATCH).transpose(0, 1, 3, 2, 4).reshape(QUADS, P, 2, BATCH))
    xT = xT.reshape(FIELDS * DIM, BATCH)

    pair_of = {(int(i), int(j)): p for p, (i, j) in enumerate(zip(*np.triu_indices(FIELDS, k=1)))}
    w = np.zeros((ROUNDS, GROUPS, DIM, 2 * GROUP, P), W.dtype)
    place = np.zeros(PAIRS, np.int64)
    for u in range(ROUNDS):
        for m in range(GROUPS):
            for n, (i, js, row) in enumerate(group_blocks(u, m)):
                for a, (j, e, size) in enumerate(js):
                    p = pair_of[min(i, j), max(i, j)]
                    w_ij = W[p] if i < j else W[p].T
                    w[u, m, :, n, size * a:size * (a + 1)] = w_ij[:, e:e + size]
                    place[p] = P * u + row + a
    w = w.reshape(ROUNDS * GROUPS, DIM, GCOLS)

    nc = bacc.Bacc("TRN2", target_bir_lowering=False, num_devices=1)
    xT_dram = nc.dram_tensor("xT_dram", xT.shape, F32, kind="ExternalInput").ap()
    xq_dram = nc.dram_tensor("xq_dram", x_quads.shape, F32, kind="ExternalInput").ap()
    w_dram = nc.dram_tensor("w_dram", w.shape, F32, kind="ExternalInput").ap()
    out_dram = nc.dram_tensor("out_dram", (ALL_ROUNDS, P, HALVES, COLS), F32, kind="ExternalOutput").ap()
    bilinear_kernel(nc, xT_dram, xq_dram, w_dram, out_dram)
    r = run_bass_kernel_spmd(nc, [{"xT_dram": xT, "xq_dram": x_quads, "w_dram": w}], core_ids=[0])
    got = np.asarray(r.results[0]["out_dram"]).reshape(TILES, ROUNDS * P, TILE)
    return np.ascontiguousarray(got[:, place, :].transpose(0, 2, 1).reshape(BATCH, PAIRS))
```
